# Optimizing a Trainium2 kernel written in Bass

```python
import numpy as np
import jax
import jax.numpy as jnp

def _softmax(x, axis=-1):
    return jax.nn.softmax(x, axis=axis)

def _gelu(x):
    return jax.nn.gelu(x, approximate=True)

def _silu(x):
    return jax.nn.silu(x)

def _sigmoid(x):
    return jax.nn.sigmoid(x)

def _layernorm(x, axis=-1, eps=1e-05):
    m = jnp.mean(x, axis=axis, keepdims=True)
    v = jnp.var(x, axis=axis, keepdims=True)
    return (x - m) / jnp.sqrt(v + eps)

def _scatter_add(tgt, idx, src, axis=0):
    return tgt.at[idx].add(src)

def _segment_sum(src, seg, n):
    return jax.ops.segment_sum(src, seg, n)
kernel_name = 'mk_rec_standalone_d1_rec_r8_d2d627'

def setup_inputs(seed: int=0):
    np.random.seed(seed)
    _w = jnp.asarray

    def _rec_inputs():
        import jax
        import jax.numpy as jnp
        _rk = jax.random.key(seed)
        r_decade_idxs = jax.random.randint(jax.random.fold_in(_rk, 1), (512, 12), 0, 2, jnp.int32)
        r_movie_idxs = jax.random.randint(jax.random.fold_in(_rk, 2), (512, 7500), 0, 2, jnp.int32)
        r_category_idxs = jax.random.randint(jax.random.fold_in(_rk, 3), (512, 32), 0, 2, jnp.int32)
        r_person_idxs = jax.random.randint(jax.random.fold_in(_rk, 4), (512, 12500), 0, 2, jnp.int32)
        r_company_idxs = jax.random.randint(jax.random.fold_in(_rk, 5), (512, 2500), 0, 2, jnp.int32)
        return (r_decade_idxs, r_movie_idxs, r_category_idxs, r_person_idxs, r_company_idxs)
    r_decade_idxs, r_movie_idxs, r_category_idxs, r_person_idxs, r_company_idxs = _rec_inputs()

    def _L0_rec_setup():
        import jax, jax.numpy as jnp
        import numpy as np
        B = 256
        LF = 64
        N_DEC, N_MOV, N_CAT, N_PER, N_COM = (12, 7500, 32, 12500, 2500)

        def _norm_rows(emb, s):
            mask = s != 0
            safe = jnp.where(mask, s, jnp.ones_like(s))
            return jnp.where(mask[:, None], emb / safe[:, None], emb)
        key = jax.random.key(seed)
        ks = jax.random.split(key, 10)

        def multihot(k, n):
            return jax.random.randint(k, (B, n), 0, 2, dtype=jnp.int32)

        def weight(k, n):
            return jax.random.normal(k, (n, LF), dtype=jnp.float32) * 0.02
        return {'decade_idxs': multihot(ks[0], N_DEC), 'movie_idxs': multihot(ks[1], N_MOV), 'category_idxs': multihot(ks[2], N_CAT), 'person_idxs': multihot(ks[3], N_PER), 'company_idxs': multihot(ks[4], N_COM), 'W_dec': weight(ks[5], N_DEC), 'W_mov': weight(ks[6], N_MOV), 'W_cat': weight(ks[7], N_CAT), 'W_per': weight(ks[8], N_PER), 'W_com': weight(ks[9], N_COM)}
    _L0_rec_all = _L0_rec_setup()
    _L0_rec_in = {k: v for k, v in _L0_rec_all.items() if k in ('W_dec', 'W_mov', 'W_cat', 'W_per', 'W_com')}
    del _L0_rec_all
    return {'r_decade_idxs': r_decade_idxs, 'r_movie_idxs': r_movie_idxs, 'r_category_idxs': r_category_idxs, 'r_person_idxs': r_person_idxs, 'r_company_idxs': r_company_idxs, 'L0_rec_W_dec': _L0_rec_in['W_dec'], 'L0_rec_W_mov': _L0_rec_in['W_mov'], 'L0_rec_W_cat': _L0_rec_in['W_cat'], 'L0_rec_W_per': _L0_rec_in['W_per'], 'L0_rec_W_com': _L0_rec_in['W_com']}

def reference(r_decade_idxs, r_movie_idxs, r_category_idxs, r_person_idxs, r_company_idxs, L0_rec_W_dec, L0_rec_W_mov, L0_rec_W_cat, L0_rec_W_per, L0_rec_W_com):
    import jax
    import jax.numpy as jnp

    def _L0_rec_ref(decade_idxs, movie_idxs, category_idxs, person_idxs, company_idxs, W_dec, W_mov, W_cat, W_per, W_com):
        import jax, jax.numpy as jnp
        import numpy as np
        B = 256
        LF = 64
        N_DEC, N_MOV, N_CAT, N_PER, N_COM = (12, 7500, 32, 12500, 2500)

        def _norm_rows(emb, s):
            mask = s != 0
            safe = jnp.where(mask, s, jnp.ones_like(s))
            return jnp.where(mask[:, None], emb / safe[:, None], emb)
        d = decade_idxs.astype(jnp.float32)
        m = movie_idxs.astype(jnp.float32)
        c = category_idxs.astype(jnp.float32)
        p = person_idxs.astype(jnp.float32)
        q = company_idxs.astype(jnp.float32)
        decades = d @ W_dec
        decades = _norm_rows(decades, jnp.sum(d, axis=1))
        movies = m @ W_mov
        decades = _norm_rows(decades, jnp.sum(m, axis=1))
        categories = _norm_rows(c @ W_cat, jnp.sum(c, axis=1))
        persons = _norm_rows(p @ W_per, jnp.sum(p, axis=1))
        companies = _norm_rows(q @ W_com, jnp.sum(q, axis=1))
        return jnp.concatenate([decades, movies, categories, persons, companies], axis=1)
    y = _L0_rec_ref(r_decade_idxs, r_movie_idxs, r_category_idxs, r_person_idxs, r_company_idxs, L0_rec_W_dec, L0_rec_W_mov, L0_rec_W_cat, L0_rec_W_per, L0_rec_W_com)
    return y

_drawn_inputs = setup_inputs


def setup_inputs(seed=0):
    import zlib

    import numpy as np

    out = dict(_drawn_inputs(seed))
    spreads = {}
    factors = {'L0_rec_W_dec': 200.0, 'L0_rec_W_cat': 8.0, 'L0_rec_W_per': 200.0, 'L0_rec_W_com': 64.0}
    for name, (base, spread) in spreads.items():
        noise = np.random.default_rng([zlib.crc32(name.encode()), seed]).standard_normal(out[name].shape)
        drawn = base * np.exp(spread * noise) if base else spread * noise
        out[name] = jnp.asarray(drawn.astype(out[name].dtype))
    for name, factor in factors.items():
        out[name] = (out[name] * factor).astype(out[name].dtype)
    return out
```

```python
from contextlib import ExitStack

import concourse.bass as bass
from concourse import mybir

F32 = mybir.dt.float32
I32 = mybir.dt.int32
ALU = mybir.AluOpType

P = 128
BATCH = 512
FACTORS = 64
GROUP = 4
SLOTS = 4
GX = GROUP * BATCH
GW = GROUP * FACTORS

STREAMED = {"person": 12500, "company": 2500, "movie": 7500}
SMALL = {"decade": 12, "category": 32}
OUT_ORDER = ["decade", "movie", "category", "person", "company"]


def split_rows(rows):
    chunks, rest = divmod(rows, P)
    return chunks // GROUP, chunks % GROUP, rest


PLAN = {name: split_rows(rows) for name, rows in STREAMED.items()}
N_GROUPS = sum(g for g, _, _ in PLAN.values())
HEAD_AT = {}
_at = 0
for _name, (_, _extra, _) in PLAN.items():
    HEAD_AT[_name] = _at
    _at += _extra
N_HEAD = _at
SHORT = {**{name: rest for name, (_, _, rest) in PLAN.items()}, **SMALL}
SHORT_AT = {name: i for i, name in enumerate(SHORT)}


def build(nc, x_stream, w_stream, x_head, w_head, x_short, w_short, out):
    P_IT = PLAN["person"][0] // SLOTS
    C_IT = PLAN["company"][0] // SLOTS
    M_IT = PLAN["movie"][0] // SLOTS
    TAIL = PLAN["movie"][0] % SLOTS
    assert PLAN["person"][0] % SLOTS == 0 and C_IT == 1 and PLAN["company"][0] % SLOTS == 0 and TAIL == 2
    LOOPS = P_IT + C_IT + M_IT

    with ExitStack() as ctx:
        def sb(name, shape, dt=F32):
            return ctx.enter_context(nc.sbuf_tensor(name, shape, dt))

        def sem(name):
            return ctx.enter_context(nc.semaphore(name))

        idx_ring = sb("idx_ring", [P, SLOTS, GX], I32)
        idxf_ring = sb("idxf_ring", [P, SLOTS, GX])
        w_ring = sb("w_ring", [P, SLOTS, GW])
        idx_head = sb("idx_head", [P, N_HEAD * BATCH], I32)
        idxf_head = sb("idxf_head", [P, N_HEAD * BATCH])
        w_head_sb = sb("w_head_sb", [P, N_HEAD * FACTORS])
        idx_short = sb("idx_short", [P, len(SHORT), BATCH], I32)
        idxf_short = sb("idxf_short", [P, len(SHORT), BATCH])
        w_short_sb = sb("w_short_sb", [P, len(SHORT), FACTORS])
        ones = sb("ones", [P, FACTORS])
        running = {name: sb(f"running_{name}", [P, GX]) for name in PLAN}
        upper = sb("upper", [FACTORS, BATCH])
        emb = {name: sb(f"emb_{name}", [FACTORS, BATCH]) for name in PLAN}
        is_zero = sb("is_zero", [P, BATCH])
        safe = sb("safe", [P, BATCH])
        inverse = sb("inverse", [P, BATCH])
        small_out = sb("small_out", [P, BATCH])
        decade_out = sb("decade_out", [FACTORS, BATCH])
        normed = {name: sb(f"normed_{name}", [FACTORS, BATCH]) for name in ("person", "company")}

        def psum(name):
            return ctx.enter_context(nc.psum_tensor(name, [P, BATCH], F32))

        emb_ps = {name: psum(f"emb_ps_{name}") for name in PLAN}
        sum_ps = {name: psum(f"sum_ps_{name}") for name in PLAN}
        small_ps = psum("small_ps")
        small_sum_ps = psum("small_sum_ps")

        idx_loaded = [sem(f"idx_loaded_{s}") for s in range(SLOTS)]
        w_loaded = [sem(f"w_loaded_{s}") for s in range(SLOTS)]
        idx_head_loaded = sem("idx_head_loaded")
        w_head_loaded = sem("w_head_loaded")
        w_short_loaded = sem("w_short_loaded")
        idx_short_loaded = {name: sem(f"idx_short_loaded_{name}") for name in SHORT}
        cleared = sem("cleared")
        head_converted = sem("head_converted")
        converted = sem("converted")
        head_summed = sem("head_summed")
        summed = sem("summed")
        products = sem("products")
        folded = sem("folded")
        row_sums = sem("row_sums")
        upper_copied = sem("upper_copied")
        upper_used = sem("upper_used")
        step = sem("step")
        finished = {name: sem(f"finished_{name}") for name in OUT_ORDER}
        stored = sem("stored")

        block = ctx.enter_context(nc.Block())

        def out_rows(name):
            at = OUT_ORDER.index(name) * FACTORS
            return out[at:at + FACTORS, :]

        @block.sync
        def _(sp):
            def load(n, s):
                sp.dma_start(w_ring[:, s, :], w_stream[n].rearrange("o p w -> (o p) w")).then_inc(w_loaded[s], 16)
                sp.dma_start(idx_ring[:, s, :], x_stream[n].rearrange("o p x -> (o p) x")).then_inc(idx_loaded[s], 16)

            def reload(g, s):
                sp.wait_ge(products, g + 1 - SLOTS)
                sp.wait_ge(summed, g + 1 - SLOTS)
                load(bass.ds(g, 1), s)

            sp.dma_start(idx_head[:], x_head).then_inc(idx_head_loaded, 16)
            sp.dma_start(w_head_sb[:], w_head).then_inc(w_head_loaded, 16)
            for s in range(SLOTS):
                load(bass.ds(s, 1), s)
            with sp.Fori(1, LOOPS) as it:
                for s in range(SLOTS):
                    reload(it * SLOTS + s, s)
            for s in range(TAIL):
                reload(LOOPS * SLOTS + s, s)
            sp.wait_ge(finished["category"], 1)
            sp.dma_start(out_rows("category"), small_out[FACTORS:P, :]).then_inc(stored, 16)
            for name in ("person", "company"):
                sp.wait_ge(finished[name], 1)
                sp.dma_start(out_rows(name), normed[name][:]).then_inc(stored, 16)
            sp.wait_ge(finished["movie"], 1)
            sp.dma_start(out_rows("movie"), emb["movie"][:]).then_inc(stored, 16)
            sp.wait_ge(finished["decade"], 1)
            sp.dma_start(out_rows("decade"), decade_out[:]).then_inc(stored, 16)
            sp.wait_ge(stored, 16 * len(OUT_ORDER))

        @block.gpsimd
        def _(pool):
            for name, rows in SHORT.items():
                i = SHORT_AT[name]
                pool.dma_start(idx_short[0:rows, i, :], x_short[name]).then_inc(idx_short_loaded[name], 16)
                pool.dma_start(w_short_sb[0:rows, i, :], w_short[name]).then_inc(w_short_loaded, 16)
            nc.gpsimd.memset(ones[:], 1.0).then_inc(cleared, 1)
            for name in PLAN:
                nc.gpsimd.memset(running[name][:], 0.0).then_inc(cleared, 1)

            groups = 0
            steps = 0
            for name in PLAN:
                groups += PLAN[name][0]
                pool.wait_ge(summed, groups)
                width = GX
                while width > BATCH:
                    width //= 2
                    r = running[name]
                    nc.gpsimd.tensor_tensor(r[:, 0:width], r[:, 0:width], r[:, width:2 * width],
                                            ALU.add).then_inc(folded, 1)
                    steps += 1
                    pool.wait_ge(folded, steps)

        @block.scalar
        def _(act):
            act.wait_ge(idx_head_loaded, 16)
            nc.scalar.copy(idxf_head[:], idx_head[:]).then_inc(head_converted, 1)
            for name, rows in SHORT.items():
                i = SHORT_AT[name]
                act.wait_ge(idx_short_loaded[name], 16)
                nc.scalar.copy(idxf_short[0:rows, i, :], idx_short[0:rows, i, :]).then_inc(head_converted, 1)

            def convert(it, s):
                act.wait_ge(idx_loaded[s], 16 * it + 16)
                if not isinstance(it, int) or it > 0:
                    act.wait_ge(products, 1 - SLOTS + it * SLOTS + s)
                nc.scalar.copy(idxf_ring[:, s, :], idx_ring[:, s, :]).then_inc(converted, 1)

            def copy_upper(name, n, groups):
                act.wait_ge(products, groups)
                if n > 0:
                    act.wait_ge(upper_used, n)
                nc.scalar.copy(upper[:], emb_ps[name][FACTORS:P, :]).then_inc(upper_copied, 1)

            for s in range(SLOTS):
                convert(0, s)
            with act.Fori(1, P_IT) as it:
                for s in range(SLOTS):
                    convert(it, s)
            for s in range(SLOTS):
                convert(P_IT, s)
                if s == 1:
                    copy_upper("person", 0, P_IT * SLOTS)
            with act.Fori(P_IT + C_IT, LOOPS) as it:
                for s in range(SLOTS):
                    convert(it, s)
            for s in range(TAIL):
                convert(LOOPS, s)
            copy_upper("company", 1, (P_IT + C_IT) * SLOTS)
            copy_upper("movie", 2, N_GROUPS)

        @block.vector
        def _(dve):
            steps = [0]

            def then(ins):
                steps[0] += 1
                ins.then_inc(step, 1)
                dve.wait_ge(step, steps[0])

            def invert(sums, parts):
                then(nc.vector.tensor_scalar(is_zero[0:parts, :], sums[0:parts, :], 0.0, None, ALU.is_equal))
                then(nc.vector.tensor_tensor(safe[0:parts, :], sums[0:parts, :], is_zero[0:parts, :], ALU.add))
                then(nc.vector.reciprocal(inverse[0:parts, :], safe[0:parts, :]))

            def join_halves(name, n):
                dve.wait_ge(upper_copied, n + 1)
                return nc.vector.tensor_tensor(emb[name][:], emb_ps[name][0:FACTORS, :], upper[:], ALU.add)

            dve.wait_ge(cleared, 1 + len(PLAN))
            dve.wait_ge(idx_head_loaded, 16)
            for name, (_, extra, rest) in PLAN.items():
                a = HEAD_AT[name] * BATCH
                r = running[name]
                nc.vector.tensor_tensor(r[:, 0:extra * BATCH], r[:, 0:extra * BATCH],
                                        idx_head[:, a:a + extra * BATCH], ALU.add).then_inc(head_summed, 1)
                dve.wait_ge(idx_short_loaded[name], 16)
                own = r[0:rest, extra * BATCH:(extra + 1) * BATCH]
                nc.vector.tensor_tensor(own, own, idx_short[0:rest, SHORT_AT[name], :],
                                        ALU.add).then_inc(head_summed, 1)

            def add_group(name, it, s):
                dve.wait_ge(idx_loaded[s], 16 * it + 16)
                if not isinstance(it, int) or it * SLOTS + s > 0:
                    dve.wait_ge(summed, it * SLOTS + s)
                nc.vector.tensor_tensor(running[name][:], running[name][:], idx_ring[:, s, :],
                                        ALU.add).then_inc(summed, 1)

            def finish_small():
                dve.wait_ge(row_sums, 1)
                invert(small_sum_ps, P)
                nc.vector.tensor_tensor(small_out[:], small_ps[:], inverse[:],
                                        ALU.mult).then_inc(finished["category"], 1)

            def finish(name, n):
                ins = join_halves(name, n)
                ins.then_inc(upper_used, 1)
                dve.wait_ge(row_sums, n + 2)
                invert(sum_ps[name], FACTORS)
                dve.wait_ge(upper_used, n + 1)
                nc.vector.tensor_tensor(normed[name][:], emb[name][:], inverse[0:FACTORS, :],
                                        ALU.mult).then_inc(finished[name], 1)

            dve.wait_ge(head_summed, 2 * len(PLAN))
            for s in range(SLOTS):
                add_group("person", 0, s)
            with dve.Fori(1, P_IT) as it:
                for s in range(SLOTS):
                    add_group("person", it, s)
            finish_small()
            for s in range(SLOTS):
                add_group("company", P_IT, s)
            dve.wait_ge(finished["category"], 1)
            finish("person", 0)
            with dve.Fori(P_IT + C_IT, LOOPS) as it:
                for s in range(SLOTS):
                    add_group("movie", it, s)
            for s in range(TAIL):
                add_group("movie", LOOPS, s)
            dve.wait_ge(finished["person"], 1)
            finish("company", 1)
            join_halves("movie", 2).then_inc(finished["movie"], 1)
            dve.wait_ge(row_sums, 4)
            dve.wait_ge(finished["company"], 1)
            invert(sum_ps["movie"], FACTORS)
            nc.vector.tensor_tensor(decade_out[:], small_out[0:FACTORS, :], inverse[0:FACTORS, :],
                                    ALU.mult).then_inc(finished["decade"], 1)

        @block.tensor
        def _(pe):
            def half(ps, c):
                return ps[(c % 2) * FACTORS:(c % 2 + 1) * FACTORS, :]

            pe.wait_ge(w_head_loaded, 16)
            pe.wait_ge(w_short_loaded, 16 * len(SHORT))
            pe.wait_ge(head_converted, 1 + len(SHORT))
            for name, (_, extra, rest) in PLAN.items():
                for c in range(extra):
                    h = HEAD_AT[name] + c
                    nc.tensor.matmul(half(emb_ps[name], c), w_head_sb[:, h * FACTORS:(h + 1) * FACTORS],
                                     idxf_head[:, h * BATCH:(h + 1) * BATCH], start=(c < 2), stop=False)
                i = SHORT_AT[name]
                nc.tensor.matmul(half(emb_ps[name], extra), w_short_sb[0:rest, i, :], idxf_short[0:rest, i, :],
                                 start=(extra < 2), stop=False)
            pe.wait_ge(cleared, 1)
            for n, (name, rows) in enumerate(SMALL.items()):
                i = SHORT_AT[name]
                nc.tensor.matmul(half(small_ps, n), w_short_sb[0:rows, i, :], idxf_short[0:rows, i, :],
                                 start=True, stop=True)
                last = nc.tensor.matmul(half(small_sum_ps, n), ones[0:rows, :], idxf_short[0:rows, i, :],
                                        start=True, stop=True)
            last.then_inc(row_sums, 1)

            def multiply_group(name, it, s, close=False):
                pe.wait_ge(w_loaded[s], 16 * it + 16)
                pe.wait_ge(converted, 1 + it * SLOTS + s)
                for c in range(GROUP):
                    last = nc.tensor.matmul(half(emb_ps[name], c), w_ring[:, s, c * FACTORS:(c + 1) * FACTORS],
                                            idxf_ring[:, s, c * BATCH:(c + 1) * BATCH], start=False,
                                            stop=close and c >= GROUP - 2)
                last.then_inc(products, 1)

            def sum_rows(name, n):
                pe.wait_ge(folded, 2 * (n + 1))
                nc.tensor.matmul(sum_ps[name][0:FACTORS, :], ones[:], running[name][:, 0:BATCH],
                                 start=True, stop=True).then_inc(row_sums, 1)

            with pe.Fori(0, P_IT - 1) as it:
                for s in range(SLOTS):
                    multiply_group("person", it, s)
            for s in range(SLOTS):
                multiply_group("person", P_IT - 1, s, close=(s == SLOTS - 1))
            for s in range(SLOTS):
                multiply_group("company", P_IT, s, close=(s == SLOTS - 1))
            sum_rows("person", 0)
            with pe.Fori(P_IT + C_IT, LOOPS) as it:
                for s in range(SLOTS):
                    multiply_group("movie", it, s)
            sum_rows("company", 1)
            for s in range(TAIL):
                multiply_group("movie", LOOPS, s, close=(s == TAIL - 1))
            sum_rows("movie", 2)


def kernel(r_decade_idxs, r_movie_idxs, r_category_idxs, r_person_idxs, r_company_idxs,
           L0_rec_W_dec, L0_rec_W_mov, L0_rec_W_cat, L0_rec_W_per, L0_rec_W_com):
    import numpy as np
    import concourse.bacc as bacc
    from concourse.bass_utils import run_bass_kernel_spmd

    idx = {"person": r_person_idxs, "company": r_company_idxs, "movie": r_movie_idxs,
           "decade": r_decade_idxs, "category": r_category_idxs}
    wts = {"person": L0_rec_W_per, "company": L0_rec_W_com, "movie": L0_rec_W_mov,
           "decade": L0_rec_W_dec, "category": L0_rec_W_cat}
    arrays = {}

    def pieces(rows_by_col):
        stream, head, short = [], [], {}
        for name, (groups, extra, rest) in PLAN.items():
            a = np.asarray(rows_by_col[name])
            n = groups * GROUP * P
            stream.append(a[:n].reshape(groups, P, GROUP * a.shape[1]))
            head.append(a[n:n + extra * P].reshape(P, extra * a.shape[1]))
            short[name] = np.ascontiguousarray(a[n + extra * P:])
        for name in SMALL:
            short[name] = np.ascontiguousarray(rows_by_col[name])
        return np.concatenate(stream), np.concatenate(head, axis=1), short

    x_stream, x_head, x_short = pieces({k: np.asarray(v).T for k, v in idx.items()})
    w_stream, w_head, w_short = pieces(wts)

    nc = bacc.Bacc("TRN2", target_bir_lowering=False, num_devices=1)

    def given(name, a):
        arrays[name] = a
        return nc.dram_tensor(name, a.shape, mybir.dt.from_np(a.dtype), kind="ExternalInput").ap()

    args = [given("x_stream", x_stream), given("w_stream", w_stream),
            given("x_head", x_head), given("w_head", w_head),
            {k: given(f"x_short_{k}", v) for k, v in x_short.items()},
            {k: given(f"w_short_{k}", v) for k, v in w_short.items()}]
    out = nc.dram_tensor("out", (len(OUT_ORDER) * FACTORS, BATCH), F32, kind="ExternalOutput").ap()
    build(nc, *args, out)
    r = run_bass_kernel_spmd(nc, [arrays], core_ids=[0])
    return np.ascontiguousarray(r.results[0]["out"].T)
```

```python
from contextlib import ExitStack

import concourse.bass as bass
from concourse import mybir

F32 = mybir.dt.float32
I32 = mybir.dt.int32
ALU = mybir.AluOpType

P = 128
BATCH = 512
HALF = BATCH // 2
FACTORS = 64
GROUP = 4
SLOTS = 4
GX = GROUP * BATCH
GW = GROUP * FACTORS

STREAMED = {"person": 12500, "company": 2500, "movie": 7500}
SMALL = {"decade": 12, "category": 32}
OUT_ORDER = ["decade", "movie", "category", "person", "company"]


def split_rows(rows):
    chunks, rest = divmod(rows, P)
    return chunks // GROUP, chunks % GROUP, rest


PLAN = {name: split_rows(rows) for name, rows in STREAMED.items()}
N_GROUPS = sum(g for g, _, _ in PLAN.values())
HEAD_AT = {}
_at = 0
for _name, (_, _extra, _) in PLAN.items():
    HEAD_AT[_name] = _at
    _at += _extra
N_HEAD = _at
HEAD_ADDS = {name: sum(e + 1 for _, e, _ in list(PLAN.values())[:i + 1]) for i, name in enumerate(PLAN)}
SHORT = {**{name: rest for name, (_, _, rest) in PLAN.items()}, **SMALL}
SHORT_AT = {name: i for i, name in enumerate(SHORT)}


def build(nc, x_stream, w_stream, x_head, w_head, x_short, w_short, out):
    PERSON_ROUNDS = PLAN["person"][0] // SLOTS
    COMPANY_ROUND = PERSON_ROUNDS
    MOVIE_ROUND = COMPANY_ROUND + 1
    ROUNDS, TAIL = divmod(N_GROUPS, SLOTS)
    assert PLAN["person"][0] % SLOTS == 0 and PLAN["company"][0] == SLOTS and TAIL == 2
    LAST = N_GROUPS - 1
    TAIL_PIECES = [(0, slice(a, a + GX // 2)) for a in (0, GX // 2)]
    LAST_PIECES = [(1, slice(c * BATCH, (c + 1) * BATCH)) for c in range(GROUP)]

    with ExitStack() as ctx:
        def sb(name, shape, dt=F32):
            return ctx.enter_context(nc.sbuf_tensor(name, shape, dt))

        def psum(name, columns):
            return ctx.enter_context(nc.psum_tensor(name, [P, 512], F32))[:, 0:columns]

        def sem(name):
            return ctx.enter_context(nc.semaphore(name))

        idx_ring = sb("idx_ring", [P, SLOTS, GX], I32)
        idxf_ring = sb("idxf_ring", [P, SLOTS, GX])
        w_ring = sb("w_ring", [P, SLOTS, GW])
        idx_head = sb("idx_head", [P, N_HEAD * BATCH], I32)
        idxf_head = sb("idxf_head", [P, N_HEAD * BATCH])
        w_head_sb = sb("w_head_sb", [P, N_HEAD * FACTORS])
        idx_short = sb("idx_short", [P, len(SHORT), BATCH], I32)
        idxf_short = sb("idxf_short", [P, len(SHORT), BATCH])
        w_short_sb = sb("w_short_sb", [P, len(SHORT), FACTORS])
        ones = sb("ones", [P, FACTORS])
        running = {name: sb(f"running_{name}", [P, GX]) for name in PLAN}
        head_sum = {name: sb(f"head_sum_{name}", [P, BATCH]) for name in PLAN}
        inverse = sb("inverse", [P, 2 * HALF])
        small_out = sb("small_out", [P, 2 * HALF])
        result = {name: sb(f"result_{name}", [P, HALF]) for name in ("person", "company", "movie", "decade")}

        emb_ps = {name: psum(f"emb_ps_{name}", HALF) for name in PLAN}
        sum_ps = {name: psum(f"sum_ps_{name}", HALF) for name in PLAN}
        small_ps = psum("small_ps", 2 * HALF)
        small_sum_ps = psum("small_sum_ps", 2 * HALF)

        idx_loaded = [sem(f"idx_loaded_{s}") for s in range(SLOTS)]
        w_loaded = [sem(f"w_loaded_{s}") for s in range(SLOTS)]
        piece_loaded = [sem(f"piece_loaded_{i}") for i in range(len(TAIL_PIECES + LAST_PIECES))]
        idx_head_loaded = sem("idx_head_loaded")
        w_head_loaded = sem("w_head_loaded")
        idx_short_loaded = sem("idx_short_loaded")
        w_short_loaded = sem("w_short_loaded")
        ones_set = sem("ones_set")
        head_converted = sem("head_converted")
        converted = sem("converted")
        piece_converted = sem("piece_converted")
        summed = sem("summed")
        head_summed = sem("head_summed")
        piece_summed = sem("piece_summed")
        products = sem("products")
        folded = sem("folded")
        tail_folded = sem("tail_folded")
        row_sums = sem("row_sums")
        movie_done = sem("movie_done")
        inverted = sem("inverted")
        finished = {name: sem(f"finished_{name}") for name in OUT_ORDER}
        stored = sem("stored")

        block = ctx.enter_context(nc.Block())

        def is_first_round(r):
            return isinstance(r, int) and r == 0

        @block.sync
        def _(sp):
            def load_w(g, s):
                sp.dma_start(w_ring[:, s, :], w_stream[bass.ds(g, 1)].rearrange("o p w -> (o p) w")
                             ).then_inc(w_loaded[s], 16)

            def load(g, s):
                load_w(g, s)
                sp.dma_start(idx_ring[:, s, :], x_stream[bass.ds(g, 1)].rearrange("o p x -> (o p) x")
                             ).then_inc(idx_loaded[s], 16)

            def wait_slot(g):
                sp.wait_ge(products, g + 1 - SLOTS)
                sp.wait_ge(summed, g + 1 - SLOTS)

            for s in range(SLOTS):
                load(s, s)
            for name, rows in SHORT.items():
                i = SHORT_AT[name]
                sp.dma_start(idx_short[0:rows, i, :], x_short[name]).then_inc(idx_short_loaded, 16)
                sp.dma_start(w_short_sb[0:rows, i, :], w_short[name]).then_inc(w_short_loaded, 16)
            sp.dma_start(w_head_sb[:], w_head).then_inc(w_head_loaded, 16)
            sp.dma_start(idx_head[:], x_head).then_inc(idx_head_loaded, 16)
            with sp.Fori(1, ROUNDS) as r:
                for s in range(SLOTS):
                    wait_slot(r * SLOTS + s)
                    load(r * SLOTS + s, s)
            for i, (s, columns) in enumerate(TAIL_PIECES + LAST_PIECES):
                if columns.start == 0:
                    wait_slot(ROUNDS * SLOTS + s)
                    load_w(ROUNDS * SLOTS + s, s)
                sp.dma_start(idx_ring[:, s, columns], x_stream[ROUNDS * SLOTS + s, :, columns]
                             ).then_inc(piece_loaded[i], 16)

            def store(name, tile):
                sp.wait_ge(finished[name], 1)
                sp.dma_start(out[OUT_ORDER.index(name)], tile).then_inc(stored, 16)

            store("category", small_out[:, HALF:2 * HALF])
            for name in ("person", "company", "decade"):
                store(name, result[name][:])
            sp.wait_ge(stored, 16 * len(OUT_ORDER))

        @block.gpsimd
        def _(pool):
            nc.gpsimd.memset(ones[:], 1.0).then_inc(ones_set, 1)

            pool.wait_ge(head_converted, 1 + len(SHORT))
            added = 0
            for name, (_, extra, rest) in PLAN.items():
                chunks = [idxf_head[:, h * BATCH:(h + 1) * BATCH]
                          for h in range(HEAD_AT[name], HEAD_AT[name] + extra)]
                total = head_sum[name]
                nc.gpsimd.tensor_copy(total[:], chunks[0]).then_inc(head_summed, 1)
                for chunk in chunks[1:]:
                    added += 1
                    pool.wait_ge(head_summed, added)
                    nc.gpsimd.tensor_tensor(total[:], total[:], chunk, ALU.add).then_inc(head_summed, 1)
                added += 1
                pool.wait_ge(head_summed, added)
                nc.gpsimd.tensor_tensor(total[0:rest, :], total[0:rest, :], idxf_short[0:rest, SHORT_AT[name], :],
                                        ALU.add).then_inc(head_summed, 1)
                added += 1

            steps = 0
            for name, groups in (("person", COMPANY_ROUND * SLOTS), ("company", MOVIE_ROUND * SLOTS)):
                pool.wait_ge(summed, groups)
                width = GX
                while width > BATCH:
                    width //= 2
                    r = running[name]
                    nc.gpsimd.tensor_tensor(r[:, 0:width], r[:, 0:width], r[:, width:2 * width],
                                            ALU.add).then_inc(folded, 1)
                    steps += 1
                    pool.wait_ge(folded, steps)

        @block.scalar
        def _(act):
            def convert(r, s):
                act.wait_ge(idx_loaded[s], 16 * r + 16)
                if not is_first_round(r):
                    act.wait_ge(products, r * SLOTS + s + 1 - SLOTS)
                nc.scalar.copy(idxf_ring[:, s, :], idx_ring[:, s, :]).then_inc(converted, 1)

            for s in range(SLOTS):
                convert(0, s)
            act.wait_ge(idx_short_loaded, 16 * len(SHORT))
            for name, rows in SHORT.items():
                i = SHORT_AT[name]
                nc.scalar.copy(idxf_short[0:rows, i, :], idx_short[0:rows, i, :]).then_inc(head_converted, 1)
            act.wait_ge(idx_head_loaded, 16)
            nc.scalar.copy(idxf_head[:], idx_head[:]).then_inc(head_converted, 1)
            with act.Fori(1, ROUNDS) as r:
                for s in range(SLOTS):
                    convert(r, s)
            for i, (s, columns) in enumerate(TAIL_PIECES + LAST_PIECES):
                if columns.start == 0:
                    act.wait_ge(products, ROUNDS * SLOTS + s + 1 - SLOTS)
                act.wait_ge(piece_loaded[i], 16)
                nc.scalar.copy(idxf_ring[:, s, columns], idx_ring[:, s, columns]).then_inc(piece_converted, 1)
            act.wait_ge(movie_done, 1)
            nc.scalar.copy(result["movie"][:], emb_ps["movie"]).then_inc(finished["movie"], 1)
            act.wait_ge(finished["movie"], 1)
            act.dma_start(out[OUT_ORDER.index("movie")], result["movie"][:]).then_inc(stored, 16)

        @block.vector
        def _(dve):
            def add_group(name, r, s, opens=False):
                g = r * SLOTS + s
                dve.wait_ge(idx_loaded[s], 16 * r + 16)
                sums = running[name][:]
                if opens:
                    nc.vector.tensor_copy(sums, idx_ring[:, s, :]).then_inc(summed, 1)
                else:
                    dve.wait_ge(summed, g)
                    nc.vector.tensor_tensor(sums, sums, idx_ring[:, s, :], ALU.add).then_inc(summed, 1)

            def divide(out_tile, features, sums, columns, done):
                nc.vector.reciprocal(inverse[:, 0:columns], sums).then_inc(inverted, 1)
                inversions[0] += 1
                dve.wait_ge(inverted, inversions[0])
                nc.vector.scalar_tensor_tensor(out=out_tile, in0=inverse[:, 0:columns], scalar=1.0, in1=features,
                                               op0=ALU.min, op1=ALU.mult).then_inc(done, 1)

            def finish(name, n):
                dve.wait_ge(row_sums, n + 1)
                divide(result[name][:], emb_ps[name], sum_ps[name], HALF, finished[name])
                dve.wait_ge(finished[name], 1)

            inversions = [0]
            for s in range(SLOTS):
                add_group("person", 0, s, opens=(s == 0))
            with dve.Fori(1, PERSON_ROUNDS) as r:
                for s in range(SLOTS):
                    add_group("person", r, s)
            for s in range(SLOTS):
                add_group("company", COMPANY_ROUND, s, opens=(s == 0))
            dve.wait_ge(row_sums, 1)
            divide(small_out[:], small_ps, small_sum_ps, 2 * HALF, finished["category"])
            dve.wait_ge(finished["category"], 1)
            for s in range(SLOTS):
                add_group("movie", MOVIE_ROUND, s, opens=(s == 0))
            finish("person", 1)
            with dve.Fori(MOVIE_ROUND + 1, ROUNDS - 1) as r:
                for s in range(SLOTS):
                    add_group("movie", r, s)
            for s in range(SLOTS):
                add_group("movie", ROUNDS - 1, s)
                if s == 0:
                    finish("company", 2)
            sums = running["movie"]
            dve.wait_ge(summed, ROUNDS * SLOTS)
            two, one = sums[:, 0:2 * BATCH], sums[:, 0:BATCH]
            nc.vector.tensor_tensor(two, two, sums[:, 2 * BATCH:4 * BATCH], ALU.add).then_inc(tail_folded, 1)
            dve.wait_ge(tail_folded, 1)
            for i, (s, columns) in enumerate(TAIL_PIECES):
                dve.wait_ge(piece_loaded[i], 16)
                if i > 0:
                    dve.wait_ge(piece_summed, i)
                nc.vector.tensor_tensor(two, two, idx_ring[:, s, columns], ALU.add).then_inc(piece_summed, 1)
            dve.wait_ge(piece_summed, len(TAIL_PIECES))
            nc.vector.tensor_tensor(one, one, sums[:, BATCH:2 * BATCH], ALU.add).then_inc(tail_folded, 1)
            dve.wait_ge(row_sums, 4)
            divide(result["decade"][:], small_out[:, 0:HALF], sum_ps["movie"], HALF, finished["decade"])

        @block.tensor
        def _(pe):
            def multiply(ps, weights, idx, start=False, stop=False):
                for h in range(2):
                    last = nc.tensor.matmul(ps[h * FACTORS:(h + 1) * FACTORS, :], weights,
                                            idx[:, h * HALF:(h + 1) * HALF], start=start, stop=stop)
                return last

            def multiply_group(name, r, s, opens=False):
                pe.wait_ge(w_loaded[s], 16 * r + 16)
                pe.wait_ge(converted, r * SLOTS + s + 1)
                for c in range(GROUP):
                    last = multiply(emb_ps[name], w_ring[:, s, c * FACTORS:(c + 1) * FACTORS],
                                    idxf_ring[:, s, c * BATCH:(c + 1) * BATCH], start=opens and c == 0)
                last.then_inc(products, 1)

            def multiply_head(name, adds, stop):
                pe.wait_ge(head_summed, adds)
                multiply(sum_ps[name], ones[:], head_sum[name][:], start=True)
                _, extra, rest = PLAN[name]
                for c in range(extra):
                    h = HEAD_AT[name] + c
                    multiply(emb_ps[name], w_head_sb[:, h * FACTORS:(h + 1) * FACTORS],
                             idxf_head[:, h * BATCH:(h + 1) * BATCH])
                i = SHORT_AT[name]
                multiply(emb_ps[name], w_short_sb[0:rest, i, :], idxf_short[0:rest, i, :], stop=stop)

            def sum_rows(name, n):
                pe.wait_ge(folded, 2 * (n + 1))
                multiply(sum_ps[name], ones[:], running[name][:, 0:BATCH], stop=True).then_inc(row_sums, 1)

            for s in range(SLOTS):
                multiply_group("person", 0, s, opens=(s == 0))
            pe.wait_ge(w_short_loaded, 16 * len(SHORT))
            pe.wait_ge(head_converted, 1 + len(SHORT))
            pe.wait_ge(ones_set, 1)
            for n, (name, rows) in enumerate(SMALL.items()):
                i = SHORT_AT[name]
                columns = slice(n * HALF, (n + 1) * HALF)
                multiply(small_ps[:, columns], w_short_sb[0:rows, i, :], idxf_short[0:rows, i, :],
                         start=True, stop=True)
                last = multiply(small_sum_ps[:, columns], ones[0:rows, :], idxf_short[0:rows, i, :],
                                start=True, stop=True)
            last.then_inc(row_sums, 1)
            pe.wait_ge(w_head_loaded, 16)
            with pe.Fori(1, PERSON_ROUNDS) as r:
                for s in range(SLOTS):
                    multiply_group("person", r, s)
            multiply_head("person", HEAD_ADDS["person"], stop=True)
            for s in range(SLOTS):
                multiply_group("company", COMPANY_ROUND, s, opens=(s == 0))
            multiply_head("company", HEAD_ADDS["company"], stop=True)
            sum_rows("person", 0)
            for s in range(SLOTS):
                multiply_group("movie", MOVIE_ROUND, s, opens=(s == 0))
            multiply_head("movie", HEAD_ADDS["movie"], stop=False)
            sum_rows("company", 1)
            with pe.Fori(MOVIE_ROUND + 1, ROUNDS) as r:
                for s in range(SLOTS):
                    multiply_group("movie", r, s)
            for i, (s, columns) in enumerate(TAIL_PIECES + LAST_PIECES):
                if columns.start == 0:
                    pe.wait_ge(w_loaded[s], 16 * (ROUNDS + 1))
                if i == len(TAIL_PIECES + LAST_PIECES) - 1:
                    pe.wait_ge(tail_folded, 2)
                    multiply(sum_ps["movie"], ones[:], running["movie"][:, 0:BATCH])
                pe.wait_ge(piece_converted, i + 1)
                for c in range(columns.start // BATCH, columns.stop // BATCH):
                    idx = idxf_ring[:, s, c * BATCH:(c + 1) * BATCH]
                    ends = (s, c) == (1, GROUP - 1)
                    if s == 1:
                        last_sum = multiply(sum_ps["movie"], ones[:], idx, stop=ends)
                    last = multiply(emb_ps["movie"], w_ring[:, s, c * FACTORS:(c + 1) * FACTORS], idx, stop=ends)
            last_sum.then_inc(row_sums, 1)
            last.then_inc(movie_done, 1)


def kernel(r_decade_idxs, r_movie_idxs, r_category_idxs, r_person_idxs, r_company_idxs,
           L0_rec_W_dec, L0_rec_W_mov, L0_rec_W_cat, L0_rec_W_per, L0_rec_W_com):
    import numpy as np
    import concourse.bacc as bacc
    from concourse.bass_utils import run_bass_kernel_spmd

    idx = {"person": r_person_idxs, "company": r_company_idxs, "movie": r_movie_idxs,
           "decade": r_decade_idxs, "category": r_category_idxs}
    wts = {"person": L0_rec_W_per, "company": L0_rec_W_com, "movie": L0_rec_W_mov,
           "decade": L0_rec_W_dec, "category": L0_rec_W_cat}
    arrays = {}

    def pieces(rows_by_col):
        stream, head, short = [], [], {}
        for name, (groups, extra, rest) in PLAN.items():
            a = np.asarray(rows_by_col[name])
            n = groups * GROUP * P
            stream.append(a[:n].reshape(groups, P, GROUP * a.shape[1]))
            head.append(a[n:n + extra * P].reshape(P, extra * a.shape[1]))
            short[name] = np.ascontiguousarray(a[n + extra * P:])
        for name in SMALL:
            short[name] = np.ascontiguousarray(rows_by_col[name])
        return np.concatenate(stream), np.concatenate(head, axis=1), short

    x_stream, x_head, x_short = pieces({k: np.asarray(v).T for k, v in idx.items()})
    w_stream, w_head, w_short = pieces(wts)

    nc = bacc.Bacc("TRN2", target_bir_lowering=False, num_devices=1)

    def given(name, a):
        arrays[name] = a
        return nc.dram_tensor(name, a.shape, mybir.dt.from_np(a.dtype), kind="ExternalInput").ap()

    args = [given("x_stream", x_stream), given("w_stream", w_stream),
            given("x_head", x_head), given("w_head", w_head),
            {k: given(f"x_short_{k}", v) for k, v in x_short.items()},
            {k: given(f"w_short_{k}", v) for k, v in w_short.items()}]
    out = nc.dram_tensor("out", (len(OUT_ORDER), P, HALF), F32, kind="ExternalOutput").ap()
    build(nc, *args, out)
    r = run_bass_kernel_spmd(nc, [arrays], core_ids=[0])
    blocks = r.results[0]["out"].reshape(len(OUT_ORDER), 2, FACTORS, HALF)
    return np.ascontiguousarray(blocks.transpose(1, 3, 0, 2).reshape(BATCH, len(OUT_ORDER) * FACTORS))
```

```python
from contextlib import ExitStack

import concourse.bass as bass
from concourse import mybir

F32 = mybir.dt.float32
I32 = mybir.dt.int32
ALU = mybir.AluOpType

P = 128
BATCH = 512
HALF = BATCH // 2
QUARTERS = BATCH // P
FACTORS = 64
GROUP = 4
SLOTS = 4
GX = GROUP * BATCH
GW = GROUP * FACTORS
HALF_GROUPS = (slice(0, GX // 2), slice(GX // 2, GX))

STREAMED = {"person": 12500, "company": 2500, "movie": 7500}
SMALL = {"decade": 12, "category": 32}
OUT_ORDER = ["decade", "movie", "category", "person", "company"]


def split_rows(rows):
    chunks, rest = divmod(rows, P)
    return chunks // GROUP, chunks % GROUP, rest


PLAN = {name: split_rows(rows) for name, rows in STREAMED.items()}
N_GROUPS = sum(g for g, _, _ in PLAN.values())
HEAD_AT = {}
_at = 0
for _name, (_, _extra, _) in PLAN.items():
    HEAD_AT[_name] = _at
    _at += _extra
N_HEAD = _at
HEAD_ADDS = {name: sum(e + 1 for _, e, _ in list(PLAN.values())[:i + 1]) for i, name in enumerate(PLAN)}
SHORT = {**{name: rest for name, (_, _, rest) in PLAN.items()}, **SMALL}
SHORT_AT = {name: i for i, name in enumerate(SHORT)}


def build(nc, x_stream, w_stream, x_head, w_head, x_short, w_short, out):
    PERSON_ROUNDS = PLAN["person"][0] // SLOTS
    COMPANY_ROUND = PERSON_ROUNDS
    MOVIE_ROUND = COMPANY_ROUND + 1
    LATE_ROUND = N_GROUPS // SLOTS - 1
    ROUNDS, TAIL = divmod(N_GROUPS, SLOTS)
    assert PLAN["person"][0] % SLOTS == 0 and PLAN["company"][0] == SLOTS and TAIL == 2
    TAIL_PIECES = [(0, half) for half in HALF_GROUPS]
    LAST_PIECES = [(1, slice(c * BATCH, (c + 1) * BATCH)) for c in range(GROUP)]

    LATE_ADDS = 2 * SLOTS - 1 + len(TAIL_PIECES + LAST_PIECES)

    with ExitStack() as ctx:
        def sb(name, shape, dt=F32):
            return ctx.enter_context(nc.sbuf_tensor(name, shape, dt))

        def psum(name, columns):
            return ctx.enter_context(nc.psum_tensor(name, [P, 512], F32))[:, 0:columns]

        def sem(name):
            return ctx.enter_context(nc.semaphore(name))

        idx_ring = sb("idx_ring", [P, SLOTS, GX], I32)
        idxf_ring = sb("idxf_ring", [P, SLOTS, GX])
        w_ring = sb("w_ring", [P, SLOTS, GW])
        idx_head = sb("idx_head", [P, N_HEAD * BATCH], I32)
        idxf_head = sb("idxf_head", [P, N_HEAD * BATCH])
        w_head_sb = sb("w_head_sb", [P, N_HEAD * FACTORS])
        idx_short = sb("idx_short", [P, len(SHORT), BATCH], I32)
        idxf_short = sb("idxf_short", [P, len(SHORT), BATCH])
        w_short_sb = sb("w_short_sb", [P, len(SHORT), FACTORS])
        ones = sb("ones", [P, FACTORS])
        running = {name: sb(f"running_{name}", [P, GX]) for name in PLAN}
        late = sb("late", [P, 2 * BATCH])
        head_sum = {name: sb(f"head_sum_{name}", [P, BATCH]) for name in PLAN}
        is_zero = sb("is_zero", [P, HALF])
        divisor = sb("divisor", [P, HALF])
        inverse = sb("inverse", [P, HALF])
        decade_inverse = sb("decade_inverse", [P, QUARTERS])
        movie_inverse = sb("movie_inverse", [P, QUARTERS])
        decade_mean = sb("decade_mean", [P, QUARTERS, FACTORS])
        result = {name: sb(f"result_{name}", [P, HALF]) for name in OUT_ORDER}

        emb_ps = {name: psum(f"emb_ps_{name}", HALF) for name in PLAN}
        sum_ps = {name: psum(f"sum_ps_{name}", HALF) for name in ("person", "company")}
        category_ps = psum("category_ps", 2 * HALF)
        emb_ps["category"], sum_ps["category"] = category_ps[:, 0:HALF], category_ps[:, HALF:2 * HALF]
        decade_ps = psum("decade_ps", QUARTERS * (FACTORS + 1))
        decade_emb_ps = decade_ps[:, 0:QUARTERS * FACTORS].rearrange("p (j f) -> p j f", j=QUARTERS)
        decade_sum_ps = decade_ps[:, QUARTERS * FACTORS:QUARTERS * (FACTORS + 1)]
        movie_sum_ps = psum("movie_sum_ps", QUARTERS)

        idx_loaded = [sem(f"idx_loaded_{s}") for s in range(SLOTS)]
        w_loaded = [sem(f"w_loaded_{s}") for s in range(SLOTS)]
        piece_loaded = [sem(f"piece_loaded_{i}") for i in range(len(TAIL_PIECES + LAST_PIECES))]
        idx_head_loaded = sem("idx_head_loaded")
        w_head_loaded = sem("w_head_loaded")
        idx_short_loaded = sem("idx_short_loaded")
        w_short_loaded = sem("w_short_loaded")
        ones_set = sem("ones_set")
        movie_sum_cleared = sem("movie_sum_cleared")
        head_converted = sem("head_converted")
        converted = sem("converted")
        piece_converted = sem("piece_converted")
        summed = sem("summed")
        head_summed = sem("head_summed")
        late_summed = sem("late_summed")
        products = sem("products")
        folded = sem("folded")
        row_sums = sem("row_sums")
        movie_done = sem("movie_done")
        step = sem("step")
        decades_scaled = sem("decades_scaled")
        finished = {name: sem(f"finished_{name}") for name in OUT_ORDER}
        stored = sem("stored")

        block = ctx.enter_context(nc.Block())

        def is_first_round(r):
            return isinstance(r, int) and r == 0

        @block.sync
        def _(sp):
            def load_w(g, s):
                sp.dma_start(w_ring[:, s, :], w_stream[bass.ds(g, 1)].rearrange("o p w -> (o p) w")
                             ).then_inc(w_loaded[s], 16)

            def load(g, s):
                load_w(g, s)
                sp.dma_start(idx_ring[:, s, :], x_stream[bass.ds(g, 1)].rearrange("o p x -> (o p) x")
                             ).then_inc(idx_loaded[s], 16)

            def wait_slot(g):
                sp.wait_ge(products, g + 1 - SLOTS)
                if isinstance(g, int) and g - SLOTS >= LATE_ROUND * SLOTS:
                    sp.wait_ge(late_summed, 1 + 2 * (g - SLOTS - LATE_ROUND * SLOTS))
                else:
                    sp.wait_ge(summed, g + 1 - SLOTS)

            for s in range(SLOTS):
                load(s, s)
            for name, rows in SHORT.items():
                i = SHORT_AT[name]
                sp.dma_start(idx_short[0:rows, i, :], x_short[name]).then_inc(idx_short_loaded, 16)
                sp.dma_start(w_short_sb[0:rows, i, :], w_short[name]).then_inc(w_short_loaded, 16)
            sp.dma_start(w_head_sb[:], w_head).then_inc(w_head_loaded, 16)
            sp.dma_start(idx_head[:], x_head).then_inc(idx_head_loaded, 16)
            with sp.Fori(1, ROUNDS) as r:
                for s in range(SLOTS):
                    wait_slot(r * SLOTS + s)
                    load(r * SLOTS + s, s)
            for i, (s, columns) in enumerate(TAIL_PIECES + LAST_PIECES):
                if columns.start == 0:
                    wait_slot(ROUNDS * SLOTS + s)
                    load_w(ROUNDS * SLOTS + s, s)
                sp.dma_start(idx_ring[:, s, columns], x_stream[ROUNDS * SLOTS + s, :, columns]
                             ).then_inc(piece_loaded[i], 16)

            def store(name, tile):
                sp.wait_ge(finished[name], 1)
                sp.dma_start(out[OUT_ORDER.index(name)], tile).then_inc(stored, 16)

            for name in ("category", "person", "company", "decade"):
                store(name, result[name][:])
            sp.wait_ge(stored, 16 * len(OUT_ORDER))

        @block.gpsimd
        def _(pool):
            nc.gpsimd.memset(ones[:], 1.0).then_inc(ones_set, 1)
            nc.gpsimd.memset(running["movie"][:], 0.0).then_inc(movie_sum_cleared, 1)

            pool.wait_ge(head_converted, 1 + len(SHORT))
            added = 0
            for name, (_, extra, rest) in PLAN.items():
                chunks = [idxf_head[:, h * BATCH:(h + 1) * BATCH]
                          for h in range(HEAD_AT[name], HEAD_AT[name] + extra)]
                total = head_sum[name]
                nc.gpsimd.tensor_copy(total[:], chunks[0]).then_inc(head_summed, 1)
                for chunk in chunks[1:]:
                    added += 1
                    pool.wait_ge(head_summed, added)
                    nc.gpsimd.tensor_tensor(total[:], total[:], chunk, ALU.add).then_inc(head_summed, 1)
                added += 1
                pool.wait_ge(head_summed, added)
                nc.gpsimd.tensor_tensor(total[0:rest, :], total[0:rest, :], idxf_short[0:rest, SHORT_AT[name], :],
                                        ALU.add).then_inc(head_summed, 1)
                added += 1

            steps = 0
            for name, groups in (("person", COMPANY_ROUND * SLOTS), ("company", MOVIE_ROUND * SLOTS),
                                 ("movie", LATE_ROUND * SLOTS)):
                pool.wait_ge(summed, groups)
                width = GX
                while width > BATCH:
                    width //= 2
                    r = running[name]
                    nc.gpsimd.tensor_tensor(r[:, 0:width], r[:, 0:width], r[:, width:2 * width],
                                            ALU.add).then_inc(folded, 1)
                    steps += 1
                    pool.wait_ge(folded, steps)

        @block.scalar
        def _(act):
            def convert(r, s):
                act.wait_ge(idx_loaded[s], 16 * r + 16)
                if not is_first_round(r):
                    act.wait_ge(products, r * SLOTS + s + 1 - SLOTS)
                for half in HALF_GROUPS:
                    nc.scalar.copy(idxf_ring[:, s, half], idx_ring[:, s, half]).then_inc(converted, 1)

            for s in range(SLOTS):
                convert(0, s)
            act.wait_ge(idx_short_loaded, 16 * len(SHORT))
            for name, rows in SHORT.items():
                i = SHORT_AT[name]
                nc.scalar.copy(idxf_short[0:rows, i, :], idx_short[0:rows, i, :]).then_inc(head_converted, 1)
            act.wait_ge(idx_head_loaded, 16)
            nc.scalar.copy(idxf_head[:], idx_head[:]).then_inc(head_converted, 1)
            with act.Fori(1, ROUNDS) as r:
                for s in range(SLOTS):
                    convert(r, s)
            for i, (s, columns) in enumerate(TAIL_PIECES + LAST_PIECES):
                if columns.start == 0:
                    act.wait_ge(products, ROUNDS * SLOTS + s + 1 - SLOTS)
                act.wait_ge(piece_loaded[i], 16)
                nc.scalar.copy(idxf_ring[:, s, columns], idx_ring[:, s, columns]).then_inc(piece_converted, 1)
            act.wait_ge(movie_done, 1)
            nc.scalar.copy(result["movie"][:], emb_ps["movie"]).then_inc(finished["movie"], 1)
            act.wait_ge(finished["movie"], 1)
            act.dma_start(out[OUT_ORDER.index("movie")], result["movie"][:]).then_inc(stored, 16)

        @block.vector
        def _(dve):
            def add_group(name, r, s, opens=False):
                dve.wait_ge(idx_loaded[s], 16 * r + 16)
                sums = running[name][:]
                if opens:
                    nc.vector.tensor_copy(sums, idx_ring[:, s, :]).then_inc(summed, 1)
                else:
                    dve.wait_ge(summed, r * SLOTS + s)
                    nc.vector.tensor_tensor(sums, sums, idx_ring[:, s, :], ALU.add).then_inc(summed, 1)

            steps = [0]

            def then(ins):
                ins.then_inc(step, 1)
                steps[0] += 1
                dve.wait_ge(step, steps[0])

            def invert(out_tile, sums):
                columns = sums.shape[1]
                then(nc.vector.tensor_scalar(is_zero[:, 0:columns], sums, 0.0, None, ALU.is_equal))
                then(nc.vector.tensor_tensor(divisor[:, 0:columns], sums, is_zero[:, 0:columns], ALU.add))
                then(nc.vector.reciprocal(out_tile, divisor[:, 0:columns]))

            def scale(out_tile, inverses, features):
                return nc.vector.tensor_tensor(out_tile, features, inverses, ALU.mult)

            def finish(name, n):
                dve.wait_ge(row_sums, n + 1)
                invert(inverse[:], sum_ps[name])
                scale(result[name][:], inverse[:], emb_ps[name]).then_inc(finished[name], 1)
                dve.wait_ge(finished[name], 1)

            def by_factor(inverses):
                return inverses.unsqueeze(2).to_broadcast([P, QUARTERS, FACTORS])

            for s in range(SLOTS):
                add_group("person", 0, s, opens=(s == 0))
            finish("category", 0)
            invert(decade_inverse[:], decade_sum_ps)
            scale(decade_mean[:], by_factor(decade_inverse[:]), decade_emb_ps).then_inc(decades_scaled, 1)
            with dve.Fori(1, PERSON_ROUNDS) as r:
                for s in range(SLOTS):
                    add_group("person", r, s)
            for s in range(SLOTS):
                add_group("company", COMPANY_ROUND, s, opens=(s == 0))
            finish("person", 1)
            dve.wait_ge(movie_sum_cleared, 1)
            with dve.Fori(MOVIE_ROUND, LATE_ROUND) as r:
                for s in range(SLOTS):
                    add_group("movie", r, s)

            lower, upper = HALF_GROUPS
            late_adds = 0
            for s in range(SLOTS):
                dve.wait_ge(idx_loaded[s], 16 * LATE_ROUND + 16)
                if s == 0:
                    nc.vector.tensor_tensor(late[:], idx_ring[:, s, lower], idx_ring[:, s, upper],
                                            ALU.add).then_inc(late_summed, 1)
                    late_adds += 1
                    finish("company", 2)
                    continue
                for half in (lower, upper):
                    dve.wait_ge(late_summed, late_adds)
                    nc.vector.tensor_tensor(late[:], late[:], idx_ring[:, s, half], ALU.add).then_inc(late_summed, 1)
                    late_adds += 1
            for i, (s, columns) in enumerate(TAIL_PIECES):
                dve.wait_ge(piece_loaded[i], 16)
                dve.wait_ge(late_summed, late_adds)
                nc.vector.tensor_tensor(late[:], late[:], idx_ring[:, s, columns], ALU.add).then_inc(late_summed, 1)
                late_adds += 1
            for c, (s, columns) in enumerate(LAST_PIECES):
                dve.wait_ge(piece_loaded[len(TAIL_PIECES) + c], 16)
                dve.wait_ge(late_summed, late_adds if c == 0 else late_adds - 1)
                sums = late[:, (c % 2) * BATCH:(c % 2 + 1) * BATCH]
                nc.vector.tensor_tensor(sums, sums, idx_ring[:, s, columns], ALU.add).then_inc(late_summed, 1)
                late_adds += 1
            assert late_adds == LATE_ADDS
            dve.wait_ge(row_sums, 4)
            invert(movie_inverse[:], movie_sum_ps)
            dve.wait_ge(decades_scaled, 1)
            scale(result["decade"][:].rearrange("p (j f) -> p j f", j=QUARTERS), by_factor(movie_inverse[:]),
                  decade_mean[:]).then_inc(finished["decade"], 1)

        @block.tensor
        def _(pe):
            def multiply(ps, weights, idx, start=False, stop=False):
                for h in range(2):
                    last = nc.tensor.matmul(ps[h * FACTORS:(h + 1) * FACTORS, :], weights,
                                            idx[:, h * HALF:(h + 1) * HALF], start=start, stop=stop)
                return last

            def sum_by_quarter(ps, idx, opens=False, closes=False):
                for j in range(QUARTERS):
                    for h in range(0, P, FACTORS):
                        last = nc.tensor.matmul(ps[h:h + FACTORS, j:j + 1], idx[:, j * P + h:j * P + h + FACTORS],
                                                ones[0:idx.shape[0], 0:1], start=opens and j == 0, stop=closes,
                                                skip_group_check=True)
                return last

            def multiply_group(name, r, s, opens=False):
                pe.wait_ge(w_loaded[s], 16 * r + 16)
                for c in range(GROUP):
                    if c % (GROUP // 2) == 0:
                        pe.wait_ge(converted, (r * SLOTS + s) * 2 + c // (GROUP // 2) + 1)
                    last = multiply(emb_ps[name], w_ring[:, s, c * FACTORS:(c + 1) * FACTORS],
                                    idxf_ring[:, s, c * BATCH:(c + 1) * BATCH], start=opens and c == 0)
                last.then_inc(products, 1)

            def multiply_head(name, adds, stop):
                pe.wait_ge(head_summed, adds)
                if name == "movie":
                    sum_by_quarter(movie_sum_ps, head_sum[name][:], opens=True)
                else:
                    multiply(sum_ps[name], ones[:], head_sum[name][:], start=True)
                _, extra, rest = PLAN[name]
                for c in range(extra):
                    h = HEAD_AT[name] + c
                    multiply(emb_ps[name], w_head_sb[:, h * FACTORS:(h + 1) * FACTORS],
                             idxf_head[:, h * BATCH:(h + 1) * BATCH], start=(name == "movie" and c == 0))
                i = SHORT_AT[name]
                multiply(emb_ps[name], w_short_sb[0:rest, i, :], idxf_short[0:rest, i, :], stop=stop)

            def sum_rows(name, n):
                pe.wait_ge(folded, 2 * (n + 1))
                multiply(sum_ps[name], ones[:], running[name][:, 0:BATCH], stop=True).then_inc(row_sums, 1)

            for s in range(SLOTS):
                multiply_group("person", 0, s, opens=(s == 0))
            pe.wait_ge(w_short_loaded, 16 * len(SHORT))
            pe.wait_ge(head_converted, len(SHORT))
            pe.wait_ge(ones_set, 1)
            i, rows = SHORT_AT["category"], SMALL["category"]
            multiply(emb_ps["category"], w_short_sb[0:rows, i, :], idxf_short[0:rows, i, :], start=True, stop=True)
            multiply(sum_ps["category"], ones[0:rows, :], idxf_short[0:rows, i, :], start=True, stop=True)
            i, rows = SHORT_AT["decade"], SMALL["decade"]
            for j in range(QUARTERS):
                nc.tensor.matmul(decade_emb_ps[:, j, :], idxf_short[0:rows, i, j * P:(j + 1) * P],
                                 w_short_sb[0:rows, i, :], start=True, stop=True)
            sum_by_quarter(decade_sum_ps, idxf_short[0:rows, i, :], opens=True, closes=True).then_inc(row_sums, 1)
            pe.wait_ge(w_head_loaded, 16)
            with pe.Fori(1, PERSON_ROUNDS) as r:
                for s in range(SLOTS):
                    multiply_group("person", r, s)
            multiply_head("person", HEAD_ADDS["person"], stop=True)
            for s in range(SLOTS):
                multiply_group("company", COMPANY_ROUND, s, opens=(s == 0))
                if s == 2:
                    sum_rows("person", 0)
            multiply_head("company", HEAD_ADDS["company"], stop=True)
            multiply_head("movie", HEAD_ADDS["movie"], stop=False)
            with pe.Fori(MOVIE_ROUND, LATE_ROUND) as r:
                for s in range(SLOTS):
                    multiply_group("movie", r, s)
            sum_rows("company", 1)
            for s in range(SLOTS):
                multiply_group("movie", LATE_ROUND, s)
                if s == 1:
                    pe.wait_ge(folded, 6)
                    sum_by_quarter(movie_sum_ps, running["movie"][:, 0:BATCH])
            for i, (s, columns) in enumerate(TAIL_PIECES + LAST_PIECES):
                if columns.start == 0:
                    pe.wait_ge(w_loaded[s], 16 * (ROUNDS + 1))
                ends = i == len(TAIL_PIECES + LAST_PIECES) - 1
                pe.wait_ge(piece_converted, i + 1)
                for c in range(columns.start // BATCH, columns.stop // BATCH):
                    last = multiply(emb_ps["movie"], w_ring[:, s, c * FACTORS:(c + 1) * FACTORS],
                                    idxf_ring[:, s, c * BATCH:(c + 1) * BATCH], stop=ends)
            last.then_inc(movie_done, 1)
            for h in range(2):
                pe.wait_ge(late_summed, LATE_ADDS - 1 + h)
                last = sum_by_quarter(movie_sum_ps, late[:, h * BATCH:(h + 1) * BATCH], closes=(h == 1))
            last.then_inc(row_sums, 1)


def kernel(r_decade_idxs, r_movie_idxs, r_category_idxs, r_person_idxs, r_company_idxs,
           L0_rec_W_dec, L0_rec_W_mov, L0_rec_W_cat, L0_rec_W_per, L0_rec_W_com):
    import numpy as np
    import concourse.bacc as bacc
    from concourse.bass_utils import run_bass_kernel_spmd

    idx = {"person": r_person_idxs, "company": r_company_idxs, "movie": r_movie_idxs,
           "decade": r_decade_idxs, "category": r_category_idxs}
    wts = {"person": L0_rec_W_per, "company": L0_rec_W_com, "movie": L0_rec_W_mov,
           "decade": L0_rec_W_dec, "category": L0_rec_W_cat}
    arrays = {}

    def pieces(rows_by_col):
        stream, head, short = [], [], {}
        for name, (groups, extra, rest) in PLAN.items():
            a = np.asarray(rows_by_col[name])
            n = groups * GROUP * P
            stream.append(a[:n].reshape(groups, P, GROUP * a.shape[1]))
            head.append(a[n:n + extra * P].reshape(P, extra * a.shape[1]))
            short[name] = np.ascontiguousarray(a[n + extra * P:])
        for name in SMALL:
            short[name] = np.ascontiguousarray(rows_by_col[name])
        return np.concatenate(stream), np.concatenate(head, axis=1), short

    x_stream, x_head, x_short = pieces({k: np.asarray(v).T for k, v in idx.items()})
    w_stream, w_head, w_short = pieces(wts)

    nc = bacc.Bacc("TRN2", target_bir_lowering=False, num_devices=1)

    def given(name, a):
        arrays[name] = a
        return nc.dram_tensor(name, a.shape, mybir.dt.from_np(a.dtype), kind="ExternalInput").ap()

    args = [given("x_stream", x_stream), given("w_stream", w_stream),
            given("x_head", x_head), given("w_head", w_head),
            {k: given(f"x_short_{k}", v) for k, v in x_short.items()},
            {k: given(f"w_short_{k}", v) for k, v in w_short.items()}]
    out = nc.dram_tensor("out", (len(OUT_ORDER), P, HALF), F32, kind="ExternalOutput").ap()
    build(nc, *args, out)
    r = run_bass_kernel_spmd(nc, [arrays], core_ids=[0])
    out = r.results[0]["out"]
    blocks = [b.reshape(2, FACTORS, HALF).transpose(0, 2, 1).reshape(BATCH, FACTORS) for b in out]
    blocks[OUT_ORDER.index("decade")] = out[OUT_ORDER.index("decade")].reshape(
        P, QUARTERS, FACTORS).transpose(1, 0, 2).reshape(BATCH, FACTORS)
    return np.concatenate(blocks, axis=1)
```
